# Optimizing a Trainium2 kernel written in Bass

```python
import numpy as np
import jax
import jax.numpy as jnp

def _softmax(x, axis=-1):
    return jax.nn.softmax(x, axis=axis)

def _gelu(x):
    return jax.nn.gelu(x, approximate=True)

def _silu(x):
    return jax.nn.silu(x)

def _sigmoid(x):
    return jax.nn.sigmoid(x)

def _layernorm(x, axis=-1, eps=1e-05):
    m = jnp.mean(x, axis=axis, keepdims=True)
    v = jnp.var(x, axis=axis, keepdims=True)
    return (x - m) / jnp.sqrt(v + eps)

def _scatter_add(tgt, idx, src, axis=0):
    return tgt.at[idx].add(src)

def _segment_sum(src, seg, n):
    return jax.ops.segment_sum(src, seg, n)
kernel_name = 'mk_dlrm_tower_d1_rec_r8_f4760c'

def setup_inputs(seed: int=0):
    np.random.seed(seed)
    _w = jnp.asarray

    def _rec_inputs():
        import jax
        import jax.numpy as jnp
        _tk = jax.random.key(seed)
        ids = jnp.stack([jax.random.randint(jax.random.fold_in(_tk, 200 + f), (2048,), 0, v, jnp.int32) for f, v in enumerate([125000, 1000, 12500, 1250, 1000, 1250, 1250, 1250, 12500, 12500, 1250, 1000, 1250, 12500, 1250, 1000, 1250, 1000, 12500, 1250, 12500, 12500, 1000, 1250, 1250, 1250])], axis=1)
        tbl_0 = 0.05 * jax.random.normal(jax.random.fold_in(_tk, 500 + 0), (125000, 128), jnp.float32)
        tbl_1 = 0.05 * jax.random.normal(jax.random.fold_in(_tk, 500 + 1), (1000, 128), jnp.float32)
        tbl_2 = 0.05 * jax.random.normal(jax.random.fold_in(_tk, 500 + 2), (12500, 128), jnp.float32)
        tbl_3 = 0.05 * jax.random.normal(jax.random.fold_in(_tk, 500 + 3), (1250, 128), jnp.float32)
        tbl_4 = 0.05 * jax.random.normal(jax.random.fold_in(_tk, 500 + 4), (1000, 128), jnp.float32)
        tbl_5 = 0.05 * jax.random.normal(jax.random.fold_in(_tk, 500 + 5), (1250, 128), jnp.float32)
        tbl_6 = 0.05 * jax.random.normal(jax.random.fold_in(_tk, 500 + 6), (1250, 128), jnp.float32)
        tbl_7 = 0.05 * jax.random.normal(jax.random.fold_in(_tk, 500 + 7), (1250, 128), jnp.float32)
        tbl_8 = 0.05 * jax.random.normal(jax.random.fold_in(_tk, 500 + 8), (12500, 128), jnp.float32)
        tbl_9 = 0.05 * jax.random.normal(jax.random.fold_in(_tk, 500 + 9), (12500, 128), jnp.float32)
        tbl_10 = 0.05 * jax.random.normal(jax.random.fold_in(_tk, 500 + 10), (1250, 128), jnp.float32)
        tbl_11 = 0.05 * jax.random.normal(jax.random.fold_in(_tk, 500 + 11), (1000, 128), jnp.float32)
        tbl_12 = 0.05 * jax.random.normal(jax.random.fold_in(_tk, 500 + 12), (1250, 128), jnp.float32)
        tbl_13 = 0.05 * jax.random.normal(jax.random.fold_in(_tk, 500 + 13), (12500, 128), jnp.float32)
        tbl_14 = 0.05 * jax.random.normal(jax.random.fold_in(_tk, 500 + 14), (1250, 128), jnp.float32)
        tbl_15 = 0.05 * jax.random.normal(jax.random.fold_in(_tk, 500 + 15), (1000, 128), jnp.float32)
        tbl_16 = 0.05 * jax.random.normal(jax.random.fold_in(_tk, 500 + 16), (1250, 128), jnp.float32)
        tbl_17 = 0.05 * jax.random.normal(jax.random.fold_in(_tk, 500 + 17), (1000, 128), jnp.float32)
        tbl_18 = 0.05 * jax.random.normal(jax.random.fold_in(_tk, 500 + 18), (12500, 128), jnp.float32)
        tbl_19 = 0.05 * jax.random.normal(jax.random.fold_in(_tk, 500 + 19), (1250, 128), jnp.float32)
        tbl_20 = 0.05 * jax.random.normal(jax.random.fold_in(_tk, 500 + 20), (12500, 128), jnp.float32)
        tbl_21 = 0.05 * jax.random.normal(jax.random.fold_in(_tk, 500 + 21), (12500, 128), jnp.float32)
        tbl_22 = 0.05 * jax.random.normal(jax.random.fold_in(_tk, 500 + 22), (1000, 128), jnp.float32)
        tbl_23 = 0.05 * jax.random.normal(jax.random.fold_in(_tk, 500 + 23), (1250, 128), jnp.float32)
        tbl_24 = 0.05 * jax.random.normal(jax.random.fold_in(_tk, 500 + 24), (1250, 128), jnp.float32)
        tbl_25 = 0.05 * jax.random.normal(jax.random.fold_in(_tk, 500 + 25), (1250, 128), jnp.float32)
        _rk = jax.random.fold_in(_tk, 7)
        r_dense_features = -0.000520686 + 1.00062 * jax.random.normal(jax.random.fold_in(_rk, 101), (2048, 128), jnp.float32)
        W_top1 = 0.0405887 * jax.random.normal(jax.random.fold_in(_tk, 801), (607, 512), jnp.float32)
        W_top2 = 0.0441942 * jax.random.normal(jax.random.fold_in(_tk, 802), (512, 256), jnp.float32)
        W_top3 = 0.0625 * jax.random.normal(jax.random.fold_in(_tk, 803), (256, 1), jnp.float32)
        b_top1 = jnp.zeros((512,), jnp.float32)
        b_top2 = jnp.zeros((256,), jnp.float32)
        return (r_dense_features, ids, tbl_0, tbl_1, tbl_2, tbl_3, tbl_4, tbl_5, tbl_6, tbl_7, tbl_8, tbl_9, tbl_10, tbl_11, tbl_12, tbl_13, tbl_14, tbl_15, tbl_16, tbl_17, tbl_18, tbl_19, tbl_20, tbl_21, tbl_22, tbl_23, tbl_24, tbl_25, W_top1, b_top1, W_top2, b_top2, W_top3)
    r_dense_features, ids, tbl_0, tbl_1, tbl_2, tbl_3, tbl_4, tbl_5, tbl_6, tbl_7, tbl_8, tbl_9, tbl_10, tbl_11, tbl_12, tbl_13, tbl_14, tbl_15, tbl_16, tbl_17, tbl_18, tbl_19, tbl_20, tbl_21, tbl_22, tbl_23, tbl_24, tbl_25, W_top1, b_top1, W_top2, b_top2, W_top3 = _rec_inputs()

    def _L0_rec_setup():
        import jax, jax.numpy as jnp
        import numpy as np
        B, F, D = (2048, 26, 128)
        key = jax.random.key(seed)
        k1, k2 = jax.random.split(key)
        dense_features = jax.random.normal(k1, (B, D), dtype=jnp.float32)
        sparse_values = jax.random.normal(k2, (B, F, D), dtype=jnp.float32)
        return {'dense_features': dense_features, 'sparse_values': sparse_values}
    _L0_rec_all = _L0_rec_setup()
    _L0_rec_in = {k: v for k, v in _L0_rec_all.items() if k in ()}
    del _L0_rec_all
    return {'r_dense_features': r_dense_features, 'ids': ids, 'tbl_0': tbl_0, 'tbl_1': tbl_1, 'tbl_2': tbl_2, 'tbl_3': tbl_3, 'tbl_4': tbl_4, 'tbl_5': tbl_5, 'tbl_6': tbl_6, 'tbl_7': tbl_7, 'tbl_8': tbl_8, 'tbl_9': tbl_9, 'tbl_10': tbl_10, 'tbl_11': tbl_11, 'tbl_12': tbl_12, 'tbl_13': tbl_13, 'tbl_14': tbl_14, 'tbl_15': tbl_15, 'tbl_16': tbl_16, 'tbl_17': tbl_17, 'tbl_18': tbl_18, 'tbl_19': tbl_19, 'tbl_20': tbl_20, 'tbl_21': tbl_21, 'tbl_22': tbl_22, 'tbl_23': tbl_23, 'tbl_24': tbl_24, 'tbl_25': tbl_25, 'W_top1': W_top1, 'b_top1': b_top1, 'W_top2': W_top2, 'b_top2': b_top2, 'W_top3': W_top3}

def reference(r_dense_features, ids, tbl_0, tbl_1, tbl_2, tbl_3, tbl_4, tbl_5, tbl_6, tbl_7, tbl_8, tbl_9, tbl_10, tbl_11, tbl_12, tbl_13, tbl_14, tbl_15, tbl_16, tbl_17, tbl_18, tbl_19, tbl_20, tbl_21, tbl_22, tbl_23, tbl_24, tbl_25, W_top1, b_top1, W_top2, b_top2, W_top3):
    import jax
    import jax.numpy as jnp

    def _L0_rec_ref(dense_features, sparse_values):
        import jax, jax.numpy as jnp
        import numpy as np
        B, F, D = (2048, 26, 128)
        sd = jnp.einsum('bfd,bd->bf', sparse_values, dense_features)
        ss = jnp.einsum('bfd,bgd->bfg', sparse_values, sparse_values)
        iu, ju = jnp.triu_indices(F, k=1)
        pairs = ss[:, iu, ju]
        return jnp.concatenate([dense_features, sd, pairs], axis=1)
    e = jnp.stack([tbl_0[ids[:, 0]], tbl_1[ids[:, 1]], tbl_2[ids[:, 2]], tbl_3[ids[:, 3]], tbl_4[ids[:, 4]], tbl_5[ids[:, 5]], tbl_6[ids[:, 6]], tbl_7[ids[:, 7]], tbl_8[ids[:, 8]], tbl_9[ids[:, 9]], tbl_10[ids[:, 10]], tbl_11[ids[:, 11]], tbl_12[ids[:, 12]], tbl_13[ids[:, 13]], tbl_14[ids[:, 14]], tbl_15[ids[:, 15]], tbl_16[ids[:, 16]], tbl_17[ids[:, 17]], tbl_18[ids[:, 18]], tbl_19[ids[:, 19]], tbl_20[ids[:, 20]], tbl_21[ids[:, 21]], tbl_22[ids[:, 22]], tbl_23[ids[:, 23]], tbl_24[ids[:, 24]], tbl_25[ids[:, 25]]], axis=1)
    z = _L0_rec_ref(r_dense_features, e)
    z = z.reshape(z.shape[0], -1)
    h = jnp.concatenate([z, r_dense_features], axis=1)
    h = jnp.maximum(h @ W_top1 + b_top1, 0.0)
    h = jnp.maximum(h @ W_top2 + b_top2, 0.0)
    y = h @ W_top3
    return y

_drawn_inputs = setup_inputs


def setup_inputs(seed=0):
    import zlib

    import numpy as np

    out = dict(_drawn_inputs(seed))
    spreads = {'b_top1': (0.0, 0.1), 'b_top2': (0.0, 0.1)}
    factors = {}
    for name, (base, spread) in spreads.items():
        noise = np.random.default_rng([zlib.crc32(name.encode()), seed]).standard_normal(out[name].shape)
        drawn = base * np.exp(spread * noise) if base else spread * noise
        out[name] = jnp.asarray(drawn.astype(out[name].dtype))
    for name, factor in factors.items():
        out[name] = (out[name] * factor).astype(out[name].dtype)
    return out
```

```python
from contextlib import ExitStack

import numpy as np

import concourse.bass as bass
from concourse import mybir

F32 = mybir.dt.float32
I32 = mybir.dt.int32
ALU = mybir.AluOpType
ACT = mybir.ActivationFunctionType

P = 128
BLOCKS = 2
NQ = 4
QP = P // NQ
QUAD = 4
CHUNK = 8
CHUNKS = QP // CHUNK


def pair_order(features):
    n = features + 1
    order = []
    for k in range(1, n // 2 + 2):
        for i in range(n - 1 if k <= n // 2 else n // 2):
            order.append((i, i + k) if i + k < n else (i + 1, i + k - n))
    return order


def dlrm_tower(nc, x, ids, tables, w_dense, w_pairs, b1, w2, b2, w3, out):
    batch, features = ids.shape
    n = features + 1
    round_samples = BLOCKS * P
    rounds = batch // round_samples
    sq = round_samples // NQ
    quads = -(-n // QUAD)
    kt_rows, kt_n, hidden1 = w_pairs.shape
    m1 = hidden1 // P
    hidden2 = w2.shape[2]
    m2 = hidden2 // P
    half = n // 2
    assert x.shape[1] == P and batch % round_samples == 0 and n <= QP and BLOCKS * quads % 2 == 0
    assert kt_rows * kt_n == n * (n - 1) // 2 and m1 == 4 and m2 == 2

    def quad_features(k):
        return range(QUAD * k, min(QUAD * k + QUAD, n))

    pair_loads, row = [], 0
    for k in range(1, half + 2):
        i, left = 0, (n - 1 if k <= half else half)
        while left:
            count = min(left, kt_rows - row % kt_rows)
            pair_loads.append((row // kt_rows, row % kt_rows, k, i, count))
            row, i, left = row + count, i + count, left - count

    gram_dram = nc.dram_tensor("gram_scratch", (n, n, round_samples), F32).ap()
    gram_flat = gram_dram.rearrange("i j s -> (i j) s")

    with ExitStack() as ctx:
        def sb(name, shape, dt=F32):
            return ctx.enter_context(nc.sbuf_tensor(name, shape, dt))

        def psum(name, shape):
            return ctx.enter_context(nc.psum_tensor(name, shape, F32))

        def sem(name):
            return ctx.enter_context(nc.semaphore(name))

        ident = sb("ident", [P, P])
        idx = [sb(f"idx{a}", [P, features], I32) for a in range(BLOCKS)]
        rows = [sb(f"rows{a}", [P, n, P]) for a in range(BLOCKS)]
        turned = [sb(f"turned{a}", [P, QP, NQ, QP]) for a in range(BLOCKS)]
        xt = sb("xt", [P, NQ, BLOCKS, QP])
        gram = sb("gram", [P, n, BLOCKS, QP])
        pairs = sb("pairs", [kt_rows, kt_n, round_samples])
        h1 = sb("h1", [P, m1, round_samples])
        h2 = sb("h2", [P, m2, round_samples])
        y_row = sb("y_row", [1, round_samples])
        wd = sb("wd", [P, 2, hidden1])
        wds = sb("wds", [P, hidden1])
        wp = sb("wp", [kt_rows, kt_n, hidden1])
        w2s = sb("w2s", [P, m1, hidden2])
        w3s = sb("w3s", [P, m2])
        b1s = sb("b1s", [P, m1])
        b2s = sb("b2s", [P, m2])

        turn_ps = [psum(f"turn_ps{b}", [P, QUAD, P]) for b in range(2)]
        gram_ps = [psum(f"gram_ps{b}", [P, CHUNK, P]) for b in range(2)]
        mlp_ps = [psum(f"mlp_ps{b}", [P, 2, round_samples]) for b in range(2)]

        ident_cleared = sem("ident_cleared")
        ident_ready = sem("ident_ready")
        pad_cleared = sem("pad_cleared")
        weights_loaded = sem("weights_loaded")
        wds_ready = sem("wds_ready")
        idx_loaded = [sem(f"idx_loaded{a}") for a in range(BLOCKS)]
        x_loaded = [sem(f"x_loaded{a}") for a in range(BLOCKS)]
        gathered = [[sem(f"gathered{a}_{k}") for k in range(quads)] for a in range(BLOCKS)]
        turned_ps = sem("turned_ps")
        turned_act = sem("turned_act")
        turned_dve = sem("turned_dve")
        xt_act = sem("xt_act")
        xt_dve = sem("xt_dve")
        gram_done = sem("gram_done")
        gram_act = sem("gram_act")
        gram_dve = sem("gram_dve")
        gram_stored = sem("gram_stored")
        pairs_loaded = sem("pairs_loaded")
        layer1_done = sem("layer1_done")
        h1_ready = sem("h1_ready")
        layer2_done = sem("layer2_done")
        h2_ready = sem("h2_ready")
        layer3_done = sem("layer3_done")
        y_ready = sem("y_ready")
        y_stored = sem("y_stored")

        per_round = BLOCKS * quads
        chunks = BLOCKS * CHUNKS
        weight_loads = 7

        def x_quad(a, k):
            return a * quads + k

        block = ctx.enter_context(nc.Block())

        @block.sync
        def _(sp):
            def load_block(r, a, first):
                if not first:
                    sp.wait_ge(turned_ps, (r - 1) * per_round + (a + 1) * quads)
                at = r * round_samples + a * P
                sp.dma_start(idx[a][:, :], ids[bass.ds(at, P), :]).then_inc(idx_loaded[a], 16)
                sp.dma_start(rows[a][:, features, :], x[bass.ds(at, P), :]).then_inc(x_loaded[a], 16)

            def bounce(r, first):
                sp.wait_ge(gram_act, (r + 1) * chunks)
                sp.wait_ge(gram_dve, (r + 1) * chunks)
                if not first:
                    sp.wait_ge(pairs_loaded, r * 16 * len(pair_loads))
                for q in range(NQ):
                    sp.dma_start(gram_dram[:, :, q * sq:(q + 1) * sq],
                                 gram[q * QP:q * QP + n, :, :, :].rearrange("i j a g -> i j (a g)")
                                 ).then_inc(gram_stored, 16)
                if not first:
                    sp.wait_ge(layer1_done, r * 2)
                sp.wait_ge(gram_stored, (r + 1) * 16 * NQ)
                for t, at, k, i, count in pair_loads:
                    start = i * (n + 1) + k
                    sp.dma_start(pairs[at:at + count, t, :],
                                 gram_flat[start:start + (count - 1) * (n + 1) + 1:n + 1, :]
                                 ).then_inc(pairs_loaded, 16)

            def store_y(r):
                sp.wait_ge(y_ready, r + 1)
                sp.dma_start(out.rearrange("b o -> o b")[:, bass.ds(r * round_samples, round_samples)],
                             y_row[:, :]).then_inc(y_stored, 16)

            for a in range(BLOCKS):
                load_block(0, a, True)
            sp.dma_start(wd[:, :, :], w_dense).then_inc(weights_loaded, 16)
            sp.dma_start(wp[:, :, :], w_pairs).then_inc(weights_loaded, 16)
            sp.dma_start(w2s[:, :, :], w2).then_inc(weights_loaded, 16)
            sp.dma_start(w3s[:, :], w3).then_inc(weights_loaded, 16)
            sp.dma_start(b1s[:, :], b1).then_inc(weights_loaded, 16)
            sp.dma_start(b2s[:, :], b2).then_inc(weights_loaded, 16)
            for a in range(BLOCKS):
                load_block(1, a, False)
            bounce(0, True)
            load_block(2, 0, False)
            store_y(0)
            load_block(2, 1, False)
            with sp.Fori(1, rounds - 2) as r:
                bounce(r, False)
                load_block(r + 2, 0, False)
                store_y(r)
                load_block(r + 2, 1, False)
            for r in range(rounds - 2, rounds):
                bounce(r, False)
                store_y(r)
            sp.wait_ge(y_stored, rounds * 16)

        @block.gpsimd
        def _(pool):
            nc.gpsimd.memset(ident[:, :], 0.0).then_inc(ident_cleared, 1)
            pool.wait_ge(ident_cleared, 1)
            nc.gpsimd.affine_select(out=ident[:, :], in_=ident[:, :], compare_op=ALU.not_equal, fill=1.0,
                                    base=0, pattern=[[-1, P]], channel_multiplier=1).then_inc(ident_ready, 1)

            expected = [pool.alloc_register(f"idx_expected{a}") for a in range(BLOCKS)]
            for a in range(BLOCKS):
                pool.reg_mov(expected[a], 16)

            def gather_round():
                for a in range(BLOCKS):
                    pool.wait_ge(idx_loaded[a], pool.snap(expected[a]))
                    pool.reg_add(expected[a], expected[a], 16)
                    for k in range(quads):
                        for f in quad_features(k):
                            if f < features:
                                nc.gpsimd.indirect_dma_start(
                                    rows[a][:, f, :], None, tables[f],
                                    bass.IndirectOffsetOnAxis(idx[a][:, f:f + 1], 0),
                                ).then_inc(gathered[a][k], 16)

            with pool.Fori(0, rounds):
                gather_round()

        @block.tensor
        def _(pe):
            def turn(r, a, k, first):
                m = x_quad(a, k)
                own = [f for f in quad_features(k) if f < features]
                pe.wait_ge(gathered[a][k], (r + 1) * 16 * len(own))
                if k == quads - 1:
                    pe.wait_ge(x_loaded[a], (r + 1) * 16)
                copied = turned_dve if m % 2 else turned_act
                if not (first and m < 2):
                    pe.wait_ge(copied, r * (per_round // 2) + m // 2)
                for j, f in enumerate(quad_features(k)):
                    last = nc.tensor.transpose(turn_ps[m % 2][:, j, :], rows[a][:, f, :], ident[:, :])
                last.then_inc(turned_ps, 1)

            def grams(r, a, first):
                done = (a + 1) * quads
                pe.wait_ge(turned_act, r * (per_round // 2) + (done + 1) // 2)
                pe.wait_ge(turned_dve, r * (per_round // 2) + done // 2)
                for c in range(CHUNKS):
                    m = a * CHUNKS + c
                    if not (first and m < 2):
                        pe.wait_ge(gram_act, r * chunks + m - 1)
                        pe.wait_ge(gram_dve, r * chunks + m - 1)
                    for g in range(CHUNK):
                        group = turned[a][:, c * CHUNK + g, :, :]
                        last = nc.tensor.matmul(gram_ps[m % 2][:, g, 0:NQ * n],
                                                group.rearrange("d q f -> d (q f)"), group[:, :, 0:n],
                                                start=True, stop=True)
                    last.then_inc(gram_done, 1)

            def mlp(r, first):
                xt_cols = xt[:, :, :, :].rearrange("d q a g -> d (q a g)")
                pe.wait_ge(xt_act, r + 1)
                pe.wait_ge(xt_dve, r + 1)
                pe.wait_ge(pairs_loaded, (r + 1) * 16 * len(pair_loads))
                for m in range(m1):
                    if not first and m == 2:
                        pe.wait_ge(y_ready, r)
                    cols = slice(m * P, (m + 1) * P)
                    o = mlp_ps[m // 2][:, m % 2, :]
                    nc.tensor.matmul(o, wds[:, cols], xt_cols, start=True, stop=False)
                    for t in range(kt_n):
                        last = nc.tensor.matmul(o, wp[:, t, cols], pairs[:, t, :],
                                                start=False, stop=(t == kt_n - 1))
                    if m % 2:
                        last.then_inc(layer1_done, 1)
                pe.wait_ge(h1_ready, (r + 1) * m1)
                for m in range(m2):
                    for t in range(m1):
                        last = nc.tensor.matmul(mlp_ps[0][:, m, :], w2s[:, t, m * P:(m + 1) * P],
                                                h1[:, t, :], start=(t == 0), stop=(t == m1 - 1))
                last.then_inc(layer2_done, 1)
                pe.wait_ge(h2_ready, (r + 1) * m2)
                for t in range(m2):
                    last = nc.tensor.matmul(mlp_ps[1][0:1, 0, :], w3s[:, t:t + 1], h2[:, t, :],
                                            start=(t == 0), stop=(t == m2 - 1))
                last.then_inc(layer3_done, 1)

            def round_(r, first, before):
                for a in range(BLOCKS):
                    for k in range(quads):
                        turn(r, a, k, first)
                        if a == 0 and k == 1 and not first:
                            mlp(r - 1, before)
                    grams(r, a, first)

            pe.wait_ge(ident_ready, 1)
            pe.wait_ge(pad_cleared, BLOCKS)
            round_(0, True, False)
            pe.wait_ge(wds_ready, 1)
            pe.wait_ge(weights_loaded, 6 * 16)
            round_(1, False, True)
            with pe.Fori(2, rounds) as r:
                round_(r, False, False)
            mlp(rounds - 1, False)

        def copy_turned(engine, copy, r, a, k):
            m = x_quad(a, k)
            count = len(quad_features(k))
            engine.wait_ge(turned_ps, r * per_round + m + 1)
            last = copy(turned[a][:, :, :, QUAD * k:QUAD * k + count].rearrange("d g q f -> d f q g"),
                        turn_ps[m % 2][:, 0:count, :].rearrange("d f (q g) -> d f q g", q=NQ))
            if k == quads - 1:
                copy(xt[:, :, a, :],
                     turn_ps[m % 2][:, count - 1, :].rearrange("d (q g) -> d q g", q=NQ)
                     ).then_inc(xt_dve if m % 2 else xt_act, 1)
            return last

        def copy_gram(engine, copy, r, a, c, quadrants, first):
            m = a * CHUNKS + c
            engine.wait_ge(gram_done, r * chunks + m + 1)
            if m == 0 and not first:
                engine.wait_ge(gram_stored, r * 16 * NQ)
            for q in quadrants:
                last = copy(gram[q * QP:q * QP + n, :, a, c * CHUNK:(c + 1) * CHUNK],
                            gram_ps[m % 2][q * QP:q * QP + n, :, q * n:(q + 1) * n]
                            .rearrange("i g j -> i j g"))
            return last

        @block.scalar
        def _(act):
            def relu(r):
                for m in range(m1):
                    if m % 2 == 0:
                        act.wait_ge(layer1_done, r * 2 + m // 2 + 1)
                    nc.scalar.activation(h1[:, m, :], mlp_ps[m // 2][:, m % 2, :], ACT.Relu,
                                         bias=b1s[:, m:m + 1]).then_inc(h1_ready, 1)
                act.wait_ge(layer2_done, r + 1)
                for m in range(m2):
                    nc.scalar.activation(h2[:, m, :], mlp_ps[0][:, m, :], ACT.Relu,
                                         bias=b2s[:, m:m + 1]).then_inc(h2_ready, 1)

            def round_(r, first):
                for a in range(BLOCKS):
                    for k in range(quads):
                        if x_quad(a, k) % 2 == 0:
                            copy_turned(act, nc.scalar.copy, r, a, k).then_inc(turned_act, 1)
                        if a == 0 and k == 1 and not first:
                            relu(r - 1)
                    for c in range(CHUNKS):
                        copy_gram(act, nc.scalar.copy, r, a, c, (0, 1), first).then_inc(gram_act, 1)

            round_(0, True)
            act.wait_ge(weights_loaded, 6 * 16)
            with act.Fori(1, rounds) as r:
                round_(r, False)
            relu(rounds - 1)

        @block.vector
        def _(dve):
            def copy_y(r, first):
                dve.wait_ge(layer3_done, r + 1)
                if not first:
                    dve.wait_ge(y_stored, r * 16)
                nc.vector.tensor_copy(
                    y_row[:, :].rearrange("o (a q g) -> o a q g", a=BLOCKS, q=NQ),
                    mlp_ps[1][0:1, 0, :].rearrange("o (q a g) -> o a q g", q=NQ, a=BLOCKS),
                ).then_inc(y_ready, 1)

            def round_(r, first, before):
                for a in range(BLOCKS):
                    for k in range(quads):
                        if x_quad(a, k) % 2 == 1:
                            copy_turned(dve, nc.vector.tensor_copy, r, a, k).then_inc(turned_dve, 1)
                        if a == 0 and k == 1 and not first:
                            copy_y(r - 1, before)
                    for c in range(CHUNKS):
                        copy_gram(dve, nc.vector.tensor_copy, r, a, c, (2, 3), first).then_inc(gram_dve, 1)

            for a in range(BLOCKS):
                nc.vector.memset(turned[a][:, :, :, n:QP], 0.0).then_inc(pad_cleared, 1)
            dve.wait_ge(weights_loaded, 6 * 16)
            nc.vector.tensor_tensor(wds[:, :], wd[:, 0, :], wd[:, 1, :], ALU.add).then_inc(wds_ready, 1)
            round_(0, True, False)
            round_(1, False, True)
            with dve.Fori(2, rounds) as r:
                round_(r, False, False)
            copy_y(rounds - 1, False)


def kernel(**inputs):
    import concourse.bacc as _bacc
    from concourse.bass_utils import run_bass_kernel_spmd as _run

    ids = np.ascontiguousarray(inputs["ids"])
    features = ids.shape[1]
    w1 = np.asarray(inputs["W_top1"])
    dense = inputs["r_dense_features"].shape[1]

    of_pair = {(f, features): dense + f for f in range(features)}
    row = dense + features
    for i in range(features):
        for j in range(i + 1, features):
            of_pair[i, j] = row
            row += 1
    order = [of_pair[min(p), max(p)] for p in pair_order(features)]
    tiles = 3
    w_pairs = w1[order].reshape(tiles, len(order) // tiles, -1).transpose(1, 0, 2)
    w_dense = np.stack([w1[:dense], w1[row:]], axis=1)
    cols = lambda v: np.asarray(v).reshape(-1, P).T

    arrays = {
        "x": inputs["r_dense_features"], "ids": ids,
        **{f"tbl_{f}": inputs[f"tbl_{f}"] for f in range(features)},
        "w_dense": w_dense, "w_pairs": w_pairs, "b1": cols(inputs["b_top1"]),
        "w2": np.asarray(inputs["W_top2"]).reshape(-1, P, 256).transpose(1, 0, 2),
        "b2": cols(inputs["b_top2"]), "w3": cols(inputs["W_top3"]),
    }
    arrays = {k: np.ascontiguousarray(v) for k, v in arrays.items()}
    nc = _bacc.Bacc("TRN2", target_bir_lowering=False, num_devices=1)
    aps = {k: nc.dram_tensor(k, v.shape, mybir.dt.from_np(v.dtype), kind="ExternalInput").ap()
           for k, v in arrays.items()}
    out = nc.dram_tensor("out", (ids.shape[0], 1), F32, kind="ExternalOutput").ap()
    dlrm_tower(nc, aps["x"], aps["ids"], [aps[f"tbl_{f}"] for f in range(features)], aps["w_dense"],
               aps["w_pairs"], aps["b1"], aps["w2"], aps["b2"], aps["w3"], out)
    r = _run(nc, [arrays], core_ids=[0])
    return r.results[0]["out"]
```

```python
from contextlib import ExitStack

import numpy as np

import concourse.bass as bass
from concourse import mybir

F32 = mybir.dt.float32
F32R = mybir.dt.float32r
I32 = mybir.dt.int32
ALU = mybir.AluOpType
ACT = mybir.ActivationFunctionType

P = 128
BLOCKS = 2
NQ = 4
QP = P // NQ
QUAD = 4
CHUNK = 8
CHUNKS = QP // CHUNK
PICKED = 7
ID_LOADS = 2
AHEAD = 3


def split_features(table_rows):
    by_rows = sorted(range(len(table_rows)), key=lambda f: (table_rows[f], f))
    return sorted(by_rows[PICKED:]), by_rows[:PICKED]


def pair_order(n):
    order = []
    for k in range(1, n // 2 + 2):
        for i in range(n - 1 if k <= n // 2 else n // 2):
            order.append((i, i + k) if i + k < n else (i + 1, i + k - n))
    return order


def tile_rows(table_rows):
    return max(d for d in range(1, P + 1) if table_rows % d == 0)


def dlrm_tower(nc, x, gather_ids, pick_ids, gather_tables, pick_tables, w_dense, w_pairs, b1, w2, b2,
               w3, out):
    batch, gathers = gather_ids.shape
    picks = pick_ids.shape[0]
    n = gathers + 1 + picks
    round_samples = BLOCKS * P
    rounds = batch // round_samples
    used = (NQ - 1) * QP + n
    sq = round_samples // NQ
    quads = -(-(gathers + 1) // QUAD)
    kt_rows, kt_n, hidden1 = w_pairs.shape
    m1 = hidden1 // P
    hidden2 = w2.shape[2]
    m2 = hidden2 // P
    half = n // 2
    ids_each = -(-picks // ID_LOADS)
    pick_rows = [tile_rows(t.shape[0]) for t in pick_tables]
    pick_tiles = [t.shape[0] // r for t, r in zip(pick_tables, pick_rows)]
    most_tiles = max(pick_tiles)
    tile_counts = sorted(set(pick_tiles))
    assert x.shape[1] == P and batch % round_samples == 0 and n <= QP and n % 2 == 1
    assert kt_rows * kt_n == n * (n - 1) // 2 and m1 == 4 and m2 == 2
    assert picks >= 2 * AHEAD > ids_each >= AHEAD and quads > CHUNKS >= m1 and rounds >= 4

    per_round = picks + BLOCKS * quads

    def quad_event(a, k):
        return picks + a * quads + k

    by_act = [e < quad_event(1, 0) for e in range(per_round)]
    act_events, dve_events = sum(by_act), per_round - sum(by_act)
    chunks = BLOCKS * CHUNKS

    def quad_columns(k):
        return range(QUAD * k, min(QUAD * k + QUAD, gathers + 1))

    pair_loads, row = [], 0
    for k in range(1, half + 2):
        i, left = 0, (n - 1 if k <= half else half)
        while left:
            count = min(left, kt_rows - row % kt_rows)
            pair_loads.append((row // kt_rows, row % kt_rows, k, i, count))
            row, i, left = row + count, i + count, left - count

    gram_dram = nc.dram_tensor("gram_scratch", (n, n, round_samples), F32).ap()
    gram_flat = gram_dram.rearrange("i j s -> (i j) s")

    with ExitStack() as ctx:
        def sb(name, shape, dt=F32):
            return ctx.enter_context(nc.sbuf_tensor(name, shape, dt))

        def psum(name, shape):
            return ctx.enter_context(nc.psum_tensor(name, shape, F32))

        def sem(name):
            return ctx.enter_context(nc.semaphore(name))

        ident = sb("ident", [P, P])
        idx = [sb(f"idx{a}", [P, gathers], I32) for a in range(BLOCKS)]
        rows = [sb(f"rows{a}", [P, gathers + 1, P]) for a in range(BLOCKS)]
        turned = [sb(f"turned{a}", [P, QP, NQ, QP]) for a in range(BLOCKS)]
        xt = sb("xt", [P, NQ, BLOCKS, QP])
        gram = sb("gram", [P, n, BLOCKS, QP])
        pairs = sb("pairs", [kt_rows, kt_n, round_samples])
        h1 = sb("h1", [P, m1, round_samples])
        h2 = sb("h2", [P, m2, round_samples])
        y_row = sb("y_row", [1, round_samples])
        wd = sb("wd", [P, 2, hidden1])
        wds = sb("wds", [P, hidden1])
        wp = sb("wp", [kt_rows, kt_n, hidden1])
        w2s = sb("w2s", [P, m1, hidden2])
        w3s = sb("w3s", [P, m2])
        b1s = sb("b1s", [P, m1])
        b2s = sb("b2s", [P, m2])
        staged = [sb(f"staged{b}", [P, most_tiles, P]) for b in range(2)]
        table_hi = [sb(f"table_hi{j}", [P, pick_tiles[j], P], F32R) for j in range(picks)]
        table_lo = [sb(f"table_lo{j}", [P, pick_tiles[j], P], F32R) for j in range(picks)]
        id_rows = [sb(f"id_rows{h}", [P, ids_each, round_samples], I32) for h in range(ID_LOADS)]
        one_hot = [sb(f"one_hot{b}", [P, most_tiles, round_samples], F32R) for b in range(AHEAD)]
        row_int = {c: sb(f"row_int{c}", [P, c], I32) for c in tile_counts}
        row_of = {c: sb(f"row_of{c}", [P, c]) for c in tile_counts}

        turn_ps = [psum(f"turn_ps{b}", [P, QUAD, P]) for b in range(2)]
        gram_ps = [psum(f"gram_ps{b}", [P, CHUNK, P]) for b in range(2)]
        mlp_ps = [psum(f"mlp_ps{b}", [P, 2, round_samples]) for b in range(2)]

        ident_cleared = sem("ident_cleared")
        ident_ready = sem("ident_ready")
        row_int_ready = sem("row_int_ready")
        row_of_ready = sem("row_of_ready")
        pad_cleared = sem("pad_cleared")
        weights_loaded = sem("weights_loaded")
        wds_ready = sem("wds_ready")
        staged_loaded = [sem(f"staged_loaded{b}") for b in range(2)]
        table_hi_ready = sem("table_hi_ready")
        table_lo_ready = sem("table_lo_ready")
        id_rows_loaded = [sem(f"id_rows_loaded{h}") for h in range(ID_LOADS)]
        one_hot_ready = sem("one_hot_ready")
        idx_loaded = [sem(f"idx_loaded{a}") for a in range(BLOCKS)]
        x_loaded = [sem(f"x_loaded{a}") for a in range(BLOCKS)]
        gathered = [[sem(f"gathered{a}_{k}") for k in range(quads)] for a in range(BLOCKS)]
        turned_ps = sem("turned_ps")
        turned_act = sem("turned_act")
        turned_dve = sem("turned_dve")
        xt_ready = [sem(f"xt_ready{a}") for a in range(BLOCKS)]
        gram_done = sem("gram_done")
        gram_act = sem("gram_act")
        gram_dve = sem("gram_dve")
        gram_stored = sem("gram_stored")
        pairs_loaded = sem("pairs_loaded")
        layer1_done = sem("layer1_done")
        h1_ready = sem("h1_ready")
        layer2_done = sem("layer2_done")
        h2_ready = sem("h2_ready")
        layer3_done = sem("layer3_done")
        y_ready = sem("y_ready")
        y_stored = sem("y_stored")

        weight_loads = 6
        block = ctx.enter_context(nc.Block())

        def bounce(engine, r, first, share=0, shares=1):
            engine.wait_ge(gram_act, (r + 1) * chunks)
            engine.wait_ge(gram_dve, (r + 1) * chunks)
            if not first:
                engine.wait_ge(pairs_loaded, r * 16 * len(pair_loads))
            for q in range(share, NQ, shares):
                engine.dma_start(gram_dram[:, :, q * sq:(q + 1) * sq],
                                 gram[q * QP:q * QP + n, :, :, :].rearrange("i j a g -> i j (a g)")
                                 ).then_inc(gram_stored, 16)
            if not first:
                engine.wait_ge(layer1_done, r * 2)
            engine.wait_ge(gram_stored, (r + 1) * 16 * NQ)
            for t, at, k, i, count in pair_loads[share::shares]:
                start = i * (n + 1) + k
                engine.dma_start(pairs[at:at + count, t, :],
                                 gram_flat[start:start + (count - 1) * (n + 1) + 1:n + 1, :]
                                 ).then_inc(pairs_loaded, 16)

        @block.sync
        def _(sp):
            def load_block(r, a, first):
                if not first:
                    sp.wait_ge(turned_ps, (r - 1) * per_round + quad_event(a, quads - 1) + 1)
                at = r * round_samples + a * P
                sp.dma_start(idx[a][:, :], gather_ids[bass.ds(at, P), :]).then_inc(idx_loaded[a], 16)
                sp.dma_start(rows[a][:, gathers, :], x[bass.ds(at, P), :]).then_inc(x_loaded[a], 16)

            def load_ids(r, h, first):
                if not first:
                    sp.wait_ge(one_hot_ready, (r - 1) * picks + min((h + 1) * ids_each, picks))
                mine = pick_ids[h * ids_each:min((h + 1) * ids_each, picks),
                                bass.ds(r * round_samples, round_samples)]
                count = mine.shape[0]
                sp.dma_start(id_rows[h][:, 0:count, :],
                             mine.unsqueeze(0).to_broadcast([P, count, round_samples])
                             ).then_inc(id_rows_loaded[h], 16)

            def load_table(j):
                if j >= 2:
                    sp.wait_ge(table_lo_ready, j - 1)
                sp.dma_start(staged[j % 2][0:pick_rows[j], 0:pick_tiles[j], :].rearrange("p t d -> p (t d)"),
                             pick_tables[j].rearrange("(p t) d -> p (t d)", p=pick_rows[j])
                             ).then_inc(staged_loaded[j % 2], 16)

            def store_y(r):
                sp.wait_ge(y_ready, r + 1)
                sp.dma_start(out.rearrange("b o -> o b")[:, bass.ds(r * round_samples, round_samples)],
                             y_row[:, :]).then_inc(y_stored, 16)

            load_block(0, 0, True)
            load_ids(0, 0, True)
            load_table(0)
            load_table(1)
            load_block(0, 1, True)
            for h in range(1, ID_LOADS):
                load_ids(0, h, True)
            for j in range(2, picks):
                load_table(j)
            for to, of in ((wd[:, :, :], w_dense), (wp[:, :, :], w_pairs), (w2s[:, :, :], w2),
                           (w3s[:, :], w3), (b1s[:, :], b1), (b2s[:, :], b2)):
                sp.dma_start(to, of).then_inc(weights_loaded, 16)
            for h in range(ID_LOADS):
                load_ids(1, h, False)
            for a in range(BLOCKS):
                load_block(1, a, False)

            def round_(r, first):
                bounce(sp, r, first)
                for h in range(ID_LOADS):
                    load_ids(r + 2, h, False)
                load_block(r + 2, 0, False)
                store_y(r)
                load_block(r + 2, 1, False)

            round_(0, True)
            with sp.Fori(1, rounds - 2) as r:
                round_(r, False)
            bounce(sp, rounds - 2, False)
            store_y(rounds - 2)
            bounce(sp, rounds - 1, False, 0, 2)
            store_y(rounds - 1)
            sp.wait_ge(y_stored, rounds * 16)

        @block.gpsimd
        def _(pool):
            nc.gpsimd.memset(ident[:, :], 0.0).then_inc(ident_cleared, 1)
            for c in tile_counts:
                nc.gpsimd.iota(row_int[c][:, :], [[1, c]], base=0, channel_multiplier=c
                               ).then_inc(row_int_ready, 1)
            pool.wait_ge(ident_cleared, 1)
            nc.gpsimd.affine_select(out=ident[:, :], in_=ident[:, :], compare_op=ALU.not_equal, fill=1.0,
                                    base=0, pattern=[[-1, P]], channel_multiplier=1).then_inc(ident_ready, 1)
            expected = [pool.alloc_register(f"idx_expected{a}") for a in range(BLOCKS)]
            for a in range(BLOCKS):
                pool.reg_mov(expected[a], 16)
            with pool.Fori(0, rounds):
                for a in range(BLOCKS):
                    pool.wait_ge(idx_loaded[a], pool.snap(expected[a]))
                    pool.reg_add(expected[a], expected[a], 16)
                    for f in range(gathers):
                        nc.gpsimd.indirect_dma_start(
                            rows[a][:, f, :], None, gather_tables[f],
                            bass.IndirectOffsetOnAxis(idx[a][:, f:f + 1], 0),
                        ).then_inc(gathered[a][f // QUAD], 16)

        @block.tensor
        def _(pe):
            def bank_free(r, e, first):
                if e < 2 and first:
                    return
                back = e - 2 if e >= 2 else max(i for i in range(per_round) if i % 2 == e % 2)
                each = act_events if by_act[back] else dve_events
                count = sum(by_act[i] == by_act[back] for i in range(back + 1))
                pe.wait_ge(turned_act if by_act[back] else turned_dve,
                           r * each + count - (0 if e >= 2 else each))

            def pick(r, j, first):
                pe.wait_ge(one_hot_ready, r * picks + j + 1)
                if first:
                    pe.wait_ge(table_lo_ready, j + 1)
                bank_free(r, j, first)
                tall = pick_rows[j]
                for t in range(pick_tiles[j]):
                    for part in (table_hi[j], table_lo[j]):
                        last = nc.tensor.matmul(
                            turn_ps[j % 2][:, 0:BLOCKS, :].rearrange("d a s -> d (a s)"),
                            part[0:tall, t, :], one_hot[j % AHEAD][0:tall, t, :],
                            start=(t == 0 and part is table_hi[j]),
                            stop=(t == pick_tiles[j] - 1 and part is table_lo[j]))
                last.then_inc(turned_ps, 1)

            def turn(r, a, k, first):
                e = quad_event(a, k)
                pe.wait_ge(gathered[a][k], (r + 1) * 16 * len([c for c in quad_columns(k) if c < gathers]))
                if k == quads - 1:
                    pe.wait_ge(x_loaded[a], (r + 1) * 16)
                bank_free(r, e, first)
                for j, c in enumerate(quad_columns(k)):
                    last = nc.tensor.transpose(turn_ps[e % 2][:, j, :], rows[a][:, c, :], ident[:, :])
                last.then_inc(turned_ps, 1)

            def block_copied(r, a):
                done = quad_event(a, quads - 1) + 1
                pe.wait_ge(turned_act, r * act_events + sum(by_act[:done]))
                if a:
                    pe.wait_ge(turned_dve, r * dve_events + done - sum(by_act[:done]))

            def grams(r, a, c, first):
                m = a * CHUNKS + c
                if not (first and m < 2):
                    pe.wait_ge(gram_act, r * chunks + m - 1)
                    pe.wait_ge(gram_dve, r * chunks + m - 1)
                for g in range(CHUNK):
                    group = turned[a][:, c * CHUNK + g, :, :]
                    last = nc.tensor.matmul(gram_ps[m % 2][0:used, g, 0:NQ * n],
                                            group.rearrange("d q f -> d (q f)")[:, 0:used],
                                            group[:, :, 0:n], start=True, stop=True)
                last.then_inc(gram_done, 1)

            def layer1(r, m, first):
                if m == 0:
                    for a in range(BLOCKS):
                        pe.wait_ge(xt_ready[a], r + 1)
                    pe.wait_ge(pairs_loaded, (r + 1) * 16 * len(pair_loads))
                if not first and m == 2:
                    pe.wait_ge(y_ready, r)
                cols = slice(m * P, (m + 1) * P)
                o = mlp_ps[m // 2][:, m % 2, :]
                nc.tensor.matmul(o, wds[:, cols], xt[:, :, :, :].rearrange("d q a g -> d (q a g)"),
                                 start=True, stop=False)
                for t in range(kt_n):
                    last = nc.tensor.matmul(o, wp[:, t, cols], pairs[:, t, :],
                                            start=False, stop=(t == kt_n - 1))
                if m % 2:
                    last.then_inc(layer1_done, 1)

            def layer2(r):
                pe.wait_ge(h1_ready, (r + 1) * m1)
                for m in range(m2):
                    for t in range(m1):
                        last = nc.tensor.matmul(mlp_ps[0][:, m, :], w2s[:, t, m * P:(m + 1) * P],
                                                h1[:, t, :], start=(t == 0), stop=(t == m1 - 1))
                last.then_inc(layer2_done, 1)

            def layer3(r):
                pe.wait_ge(h2_ready, (r + 1) * m2)
                for t in range(m2):
                    last = nc.tensor.matmul(mlp_ps[1][0:1, 0, :], w3s[:, t:t + 1], h2[:, t, :],
                                            start=(t == 0), stop=(t == m2 - 1))
                last.then_inc(layer3_done, 1)

            def round_(r, first, second):
                for j in range(picks):
                    pick(r, j, first)
                for k in range(quads):
                    if k < m1 and not first:
                        layer1(r - 1, k, second)
                    turn(r, 0, k, first)
                if not first:
                    layer2(r - 1)
                block_copied(r, 0)
                for c in range(CHUNKS):
                    grams(r, 0, c, first)
                    turn(r, 1, c, first)
                if not first:
                    layer3(r - 1)
                for k in range(CHUNKS, quads):
                    turn(r, 1, k, first)
                block_copied(r, 1)
                for c in range(CHUNKS):
                    grams(r, 1, c, first)

            pe.wait_ge(ident_ready, 1)
            pe.wait_ge(pad_cleared, BLOCKS)
            round_(0, True, False)
            pe.wait_ge(wds_ready, 1)
            pe.wait_ge(weights_loaded, weight_loads * 16)
            round_(1, False, True)
            with pe.Fori(2, rounds) as r:
                round_(r, False, False)
            for m in range(m1):
                layer1(rounds - 1, m, False)
            layer2(rounds - 1)
            layer3(rounds - 1)

        def copy_quad(engine, copy, r, a, k):
            e = quad_event(a, k)
            count = len(quad_columns(k))
            engine.wait_ge(turned_ps, r * per_round + e + 1)
            if k == quads - 1:
                copy(xt[:, :, a, :],
                     turn_ps[e % 2][:, count - 1, :].rearrange("d (q g) -> d q g", q=NQ)
                     ).then_inc(xt_ready[a], 1)
            return copy(turned[a][:, :, :, QUAD * k:QUAD * k + count].rearrange("d g q f -> d f q g"),
                        turn_ps[e % 2][:, 0:count, :].rearrange("d f (q g) -> d f q g", q=NQ))

        def copy_gram(engine, copy, r, a, c, quadrants, first):
            m = a * CHUNKS + c
            engine.wait_ge(gram_done, r * chunks + m + 1)
            if m == 0 and not first:
                engine.wait_ge(gram_stored, r * 16 * NQ)
            for q in quadrants:
                last = copy(gram[q * QP:q * QP + n, :, a, c * CHUNK:(c + 1) * CHUNK],
                            gram_ps[m % 2][q * QP:q * QP + n, :, q * n:(q + 1) * n]
                            .rearrange("i g j -> i j g"))
            return last

        @block.scalar
        def _(act):
            def relu1(r, bank):
                act.wait_ge(layer1_done, r * 2 + bank + 1)
                for m in range(2 * bank, 2 * bank + 2):
                    nc.scalar.activation(h1[:, m, :], mlp_ps[m // 2][:, m % 2, :], ACT.Relu,
                                         bias=b1s[:, m:m + 1]).then_inc(h1_ready, 1)

            def relu2(r):
                act.wait_ge(layer2_done, r + 1)
                for m in range(m2):
                    nc.scalar.activation(h2[:, m, :], mlp_ps[0][:, m, :], ACT.Relu,
                                         bias=b2s[:, m:m + 1]).then_inc(h2_ready, 1)

            def copy_picked(r, j):
                act.wait_ge(turned_ps, r * per_round + j + 1)
                for a in range(BLOCKS):
                    last = nc.scalar.copy(
                        turned[a][:, :, :, gathers + 1 + j].rearrange("d g q -> d q g"),
                        turn_ps[j % 2][:, a, :].rearrange("d (q g) -> d q g", q=NQ))
                last.then_inc(turned_act, 1)

            def after_picks(r, first):
                for k in range(quads):
                    copy_quad(act, nc.scalar.copy, r, 0, k).then_inc(turned_act, 1)
                    if k % 2 == 0 and k < m1 and not first:
                        relu1(r - 1, k // 2)
                if not first:
                    relu2(r - 1)
                for a in range(BLOCKS):
                    for c in range(CHUNKS):
                        copy_gram(act, nc.scalar.copy, r, a, c, (0, 1), first).then_inc(gram_act, 1)

            for j in range(picks):
                act.wait_ge(staged_loaded[j % 2], 16 * (j // 2 + 1))
                tall, tiles = pick_rows[j], pick_tiles[j]
                nc.scalar.copy(table_hi[j][0:tall, :, :], staged[j % 2][0:tall, 0:tiles, :]
                               ).then_inc(table_hi_ready, 1)
                if j:
                    copy_picked(0, j - 1)
            copy_picked(0, picks - 1)
            after_picks(0, True)
            act.wait_ge(weights_loaded, weight_loads * 16)
            with act.Fori(1, rounds) as r:
                for j in range(picks):
                    copy_picked(r, j)
                after_picks(r, False)
            bounce(act, rounds - 1, False, 1, 2)
            for bank in range(m1 // 2):
                relu1(rounds - 1, bank)
            relu2(rounds - 1)

        @block.vector
        def _(dve):
            def mark_rows(r, j, first):
                h = j // ids_each
                if j % ids_each == 0:
                    dve.wait_ge(id_rows_loaded[h], (r + 1) * 16)
                if j >= AHEAD:
                    dve.wait_ge(turned_ps, r * per_round + j - AHEAD + 1)
                elif not first:
                    back = max(i for i in range(picks) if i % AHEAD == j)
                    dve.wait_ge(turned_ps, (r - 1) * per_round + back + 1)
                tall = pick_rows[j]
                for t in range(pick_tiles[j]):
                    last = nc.vector.tensor_scalar(
                        one_hot[j % AHEAD][0:tall, t, :], id_rows[h][0:tall, j % ids_each, :],
                        row_of[pick_tiles[j]][0:tall, t:t + 1], None, ALU.is_equal)
                last.then_inc(one_hot_ready, 1)

            def copy_y(r, first):
                dve.wait_ge(layer3_done, r + 1)
                if not first:
                    dve.wait_ge(y_stored, r * 16)
                nc.vector.tensor_copy(
                    y_row[:, :].rearrange("o (a q g) -> o a q g", a=BLOCKS, q=NQ),
                    mlp_ps[1][0:1, 0, :].rearrange("o (q a g) -> o a q g", q=NQ, a=BLOCKS),
                ).then_inc(y_ready, 1)

            def quad(r, k):
                copy_quad(dve, nc.vector.tensor_copy, r, 1, k).then_inc(turned_dve, 1)

            def grams(r, a, c, first):
                copy_gram(dve, nc.vector.tensor_copy, r, a, c, (2, 3), first).then_inc(gram_dve, 1)

            def round_(r, first, second, last):
                if not first:
                    for j in range(AHEAD, picks):
                        mark_rows(r, j, False)
                if not last:
                    for j in range(AHEAD):
                        mark_rows(r + 1, j, False)
                for c in range(CHUNKS):
                    grams(r, 0, c, first)
                    quad(r, c)
                if not first:
                    copy_y(r - 1, second)
                for k in range(CHUNKS, quads):
                    quad(r, k)
                for c in range(CHUNKS):
                    grams(r, 1, c, first)

            dve.wait_ge(row_int_ready, len(tile_counts))
            for c in tile_counts:
                nc.vector.tensor_copy(row_of[c][:, :], row_int[c][:, :]).then_inc(row_of_ready, 1)
            for a in range(BLOCKS):
                nc.vector.memset(turned[a][:, :, :, n:QP], 0.0).then_inc(pad_cleared, 1)
            dve.wait_ge(row_of_ready, len(tile_counts))
            for j in range(picks):
                mark_rows(0, j, True)
                dve.wait_ge(table_hi_ready, j + 1)
                tall, tiles = pick_rows[j], pick_tiles[j]
                nc.vector.tensor_tensor(table_lo[j][0:tall, :, :], staged[j % 2][0:tall, 0:tiles, :],
                                        table_hi[j][0:tall, :, :], ALU.subtract).then_inc(table_lo_ready, 1)
            dve.wait_ge(weights_loaded, weight_loads * 16)
            nc.vector.tensor_tensor(wds[:, :], wd[:, 0, :], wd[:, 1, :], ALU.add).then_inc(wds_ready, 1)
            round_(0, True, False, False)
            round_(1, False, True, False)
            with dve.Fori(2, rounds - 1) as r:
                round_(r, False, False, False)
            round_(rounds - 1, False, False, True)
            copy_y(rounds - 1, False)


def kernel(**inputs):
    import concourse.bacc as _bacc
    from concourse.bass_utils import run_bass_kernel_spmd as _run

    ids = np.asarray(inputs["ids"])
    features = ids.shape[1]
    tables = [np.asarray(inputs[f"tbl_{f}"]) for f in range(features)]
    w1 = np.asarray(inputs["W_top1"])
    dense = inputs["r_dense_features"].shape[1]
    gathered, picked = split_features([t.shape[0] for t in tables])

    of_pair = {(f, features): dense + f for f in range(features)}
    row = dense + features
    for i in range(features):
        for j in range(i + 1, features):
            of_pair[i, j] = row
            row += 1
    column = [*gathered, features, *picked]
    order = [of_pair[tuple(sorted((column[i], column[j])))] for i, j in pair_order(features + 1)]
    tiles = -(-len(order) // P)

    def tiled(a, t):
        return a.reshape(t, a.shape[0] // t, -1).transpose(1, 0, 2)

    def columns(a):
        return np.asarray(a).reshape(-1, P).T

    arrays = {
        "x": inputs["r_dense_features"], "gather_ids": ids[:, gathered], "pick_ids": ids[:, picked].T,
        **{f"tbl_{f}": t for f, t in enumerate(tables)},
        "w_dense": np.stack([w1[:dense], w1[row:]], axis=1), "w_pairs": tiled(w1[order], tiles),
        "b1": columns(inputs["b_top1"]), "w2": tiled(np.asarray(inputs["W_top2"]), w1.shape[1] // P),
        "b2": columns(inputs["b_top2"]), "w3": columns(inputs["W_top3"]),
    }
    arrays = {k: np.ascontiguousarray(v) for k, v in arrays.items()}
    nc = _bacc.Bacc("TRN2", target_bir_lowering=False, num_devices=1)
    aps = {k: nc.dram_tensor(k, v.shape, mybir.dt.from_np(v.dtype), kind="ExternalInput").ap()
           for k, v in arrays.items()}
    out = nc.dram_tensor("out", (ids.shape[0], 1), F32, kind="ExternalOutput").ap()
    dlrm_tower(nc, aps["x"], aps["gather_ids"], aps["pick_ids"], [aps[f"tbl_{f}"] for f in gathered],
               [aps[f"tbl_{f}"] for f in picked], aps["w_dense"], aps["w_pairs"], aps["b1"], aps["w2"],
               aps["b2"], aps["w3"], out)
    r = _run(nc, [arrays], core_ids=[0])
    return r.results[0]["out"]
```

```python
from contextlib import ExitStack

import numpy as np

import concourse.bass as bass
from concourse import mybir

F32 = mybir.dt.float32
F32R = mybir.dt.float32r
I32 = mybir.dt.int32
ALU = mybir.AluOpType
ACT = mybir.ActivationFunctionType

P = 128
BLOCKS = 2
NQ = 4
QP = P // NQ
QUAD = 4
CHUNK = 8
CHUNKS = QP // CHUNK
PICKED = 7
ID_LOADS = 2
AHEAD = 3


def split_features(table_rows):
    by_rows = sorted(range(len(table_rows)), key=lambda f: (table_rows[f], f))
    return sorted(by_rows[PICKED:]), by_rows[:PICKED]


def pair_order(n):
    order = []
    for row in range(-n * (n - 1) // 2, 0):
        k = -(row // (n - 1))
        i = row + (n - 1) * k
        order.append((i, i + k) if i + k < n else (i + 1, i + k - n))
    return order


def tile_rows(table_rows):
    return max(d for d in range(1, P + 1) if table_rows % d == 0)


def dlrm_tower(nc, x_turned, gather_ids, pick_ids, gather_tables, pick_tables, w_dense, w_pairs, b1, w2, b2,
               w3, out):
    batch, gathers = gather_ids.shape[0], gather_ids.shape[1] - 1
    picks = pick_ids.shape[1]
    n = gathers + 1 + picks
    round_samples = BLOCKS * P
    rounds = batch // round_samples
    used = (NQ - 1) * QP + n
    sq = round_samples // NQ
    quads = -(-gathers // QUAD)
    kt_rows, kt_n, hidden1 = w_pairs.shape
    m1 = hidden1 // P
    hidden2 = w2.shape[2]
    m2 = hidden2 // P
    ids_each = -(-picks // ID_LOADS)
    pick_rows = [tile_rows(t.shape[0]) for t in pick_tables]
    pick_tiles = [t.shape[0] // r for t, r in zip(pick_tables, pick_rows)]
    most_tiles = max(pick_tiles)
    tile_counts = sorted(set(pick_tiles))
    assert x_turned.shape[1] == P and batch % round_samples == 0 and n <= QP and n % 2 == 1
    assert kt_rows * kt_n == n * (n - 1) // 2 and m1 == 4 and m2 == 2
    assert quads == 5 and quads < picks and CHUNKS == 4 and AHEAD < picks and rounds >= 5

    turns = [[("turn", a, k) for k in range(quads)] for a in range(BLOCKS)]
    lookups = [("pick", j) for j in range(picks)]
    usual = lookups + turns[0] + turns[1]
    order_0 = lookups[:1]
    for k in range(quads):
        order_0 += lookups[k + 1:k + 2] + [turns[0][k]]
    order_0 += lookups[quads + 1:] + turns[1]

    def passed(r, step, order):
        return r * len(order) + order.index(step) + 1

    chunks = BLOCKS * CHUNKS

    def quad_features(a, k):
        return range(QUAD * k, min(QUAD * k + QUAD, gathers + a))

    def pick_samples(j):
        return round_samples if j < picks - 1 else P

    row_min, row_max = -(n - 1) ** 2, n * (n - 2)
    scratch = nc.dram_tensor("gram_scratch", (row_max + 1 - row_min, round_samples), F32).ap()
    first_pair = -n * (n - 1) // 2 - row_min

    def scratch_entries(i, count_i, back_j, count_j, shift, q):
        row = n * i - (n - 1) * (n - 1 - back_j) - shift - row_min
        return bass.AP(tensor=scratch.tensor, offset=row * round_samples + q * sq,
                       ap=[[n * round_samples, count_i], [(n - 1) * round_samples, count_j], [1, sq]])

    with ExitStack() as ctx:
        def sb(name, shape, dt=F32):
            return ctx.enter_context(nc.sbuf_tensor(name, shape, dt))

        def psum(name, shape):
            return ctx.enter_context(nc.psum_tensor(name, shape, F32))

        def sem(name):
            return ctx.enter_context(nc.semaphore(name))

        ident = sb("ident", [P, P])
        idx = [sb(f"idx{a}", [P, gathers + 1], I32) for a in range(BLOCKS)]
        rows = [sb(f"rows{a}", [P, gathers + a, P]) for a in range(BLOCKS)]
        turned = [sb(f"turned{a}", [P, QP, NQ, QP]) for a in range(BLOCKS)]
        xt = sb("xt", [P, NQ, BLOCKS, QP])
        gram = sb("gram", [P, n, BLOCKS, QP])
        pairs = sb("pairs", [kt_rows, kt_n, round_samples])
        picked = sb("picked", [P, 1 + picks, BLOCKS, P])
        h1 = sb("h1", [P, m1, round_samples])
        h2 = sb("h2", [P, m2, round_samples])
        y_terms = sb("y_terms", [P, round_samples])
        ones = sb("ones", [P, 1])
        y_row = sb("y_row", [1, round_samples])
        wd = sb("wd", [P, 2, hidden1])
        wds = sb("wds", [P, hidden1])
        wp = sb("wp", [kt_rows, kt_n, hidden1])
        w2s = sb("w2s", [P, m1, hidden2])
        w3s = sb("w3s", [P, m2])
        b1s = sb("b1s", [P, m1])
        b2s = sb("b2s", [P, m2])
        staged = [sb(f"staged{b}", [P, most_tiles, P]) for b in range(2)]
        table_hi = [sb(f"table_hi{j}", [P, pick_tiles[j], P], F32R) for j in range(picks)]
        table_lo = [sb(f"table_lo{j}", [P, pick_tiles[j], P], F32R) for j in range(picks)]
        id_rows = [sb(f"id_rows{h}", [P, ids_each, round_samples], I32) for h in range(ID_LOADS)]
        one_hot = [sb(f"one_hot{b}", [P, most_tiles, round_samples], F32R) for b in range(AHEAD)]
        row_int = {c: sb(f"row_int{c}", [P, c], I32) for c in tile_counts}
        row_of = {c: sb(f"row_of{c}", [P, c]) for c in tile_counts}

        turn_ps = [psum(f"turn_ps{b}", [P, QUAD, P]) for b in range(2)]
        gram_ps = [psum(f"gram_ps{b}", [P, CHUNK, P]) for b in range(2)]
        mlp_ps = [psum(f"mlp_ps{b}", [P, 2, round_samples]) for b in range(2)]

        ident_cleared = sem("ident_cleared")
        ident_ready = sem("ident_ready")
        row_int_ready = sem("row_int_ready")
        row_of_ready = sem("row_of_ready")
        pad_cleared = sem("pad_cleared")
        ones_ready = sem("ones_ready")
        weights_loaded = sem("weights_loaded")
        wds_ready = sem("wds_ready")
        staged_loaded = [sem(f"staged_loaded{b}") for b in range(2)]
        table_hi_ready = sem("table_hi_ready")
        table_lo_ready = sem("table_lo_ready")
        id_rows_loaded = [sem(f"id_rows_loaded{h}") for h in range(ID_LOADS)]
        one_hot_ready = sem("one_hot_ready")
        idx_loaded = [sem(f"idx_loaded{a}") for a in range(BLOCKS)]
        x_loaded = sem("x_loaded")
        gathered = [[sem(f"gathered{a}_{k}") for k in range(quads)] for a in range(BLOCKS)]
        filled = sem("filled")
        emptied = sem("emptied")
        block_in = [sem(f"block_in{a}") for a in range(BLOCKS)]
        xt_ready = sem("xt_ready")
        gram_done = sem("gram_done")
        gram_act = sem("gram_act")
        gram_dve = sem("gram_dve")
        gram_stored = sem("gram_stored")
        pairs_loaded = sem("pairs_loaded")
        layer1_done = sem("layer1_done")
        h1_ready = sem("h1_ready")
        layer2_done = sem("layer2_done")
        h2_ready = sem("h2_ready")
        y_terms_ready = sem("y_terms_ready")
        layer3_done = sem("layer3_done")
        y_ready = sem("y_ready")
        y_stored = sem("y_stored")

        weight_loads = 6
        block = ctx.enter_context(nc.Block())

        upper = (0, n - 1, 0, n - 1, 0)
        lower = (n - n // 2, n // 2, n - n // 2, n // 2, n * n)
        stores = [(q, part) for part in (upper, lower) for q in range(NQ)]

        @block.sync
        def _(sp):
            def load_idx(r, a, order):
                if order:
                    sp.wait_ge(filled, passed(r - 1, turns[a][-1], order))
                sp.dma_start(idx[a][:, :], gather_ids[bass.ds(r * round_samples + a * P, P), :]
                             ).then_inc(idx_loaded[a], 16)

            def load_x(r, first):
                if not first:
                    sp.wait_ge(block_in[1], r)
                sp.dma_start(picked[:, 1, :, :], x_turned[bass.ds(r, 1), :, :]
                             .rearrange("r d (a s) -> (r d) a s", a=BLOCKS)).then_inc(x_loaded, 16)

            def load_ids(r, h, first):
                if not first:
                    sp.wait_ge(one_hot_ready, (r - 1) * picks + min((h + 1) * ids_each, picks))
                mine = pick_ids[bass.ds(r, 1), h * ids_each:min((h + 1) * ids_each, picks), :]
                mine = mine.rearrange("r f s -> (r f) s")
                count = mine.shape[0]
                sp.dma_start(id_rows[h][:, 0:count, :],
                             mine.unsqueeze(0).to_broadcast([P, count, round_samples])
                             ).then_inc(id_rows_loaded[h], 16)

            def load_table(j):
                if j >= 2:
                    sp.wait_ge(table_lo_ready, j - 1)
                sp.dma_start(staged[j % 2][0:pick_rows[j], 0:pick_tiles[j], :].rearrange("p t d -> p (t d)"),
                             pick_tables[j].rearrange("(p t) d -> p (t d)", p=pick_rows[j])
                             ).then_inc(staged_loaded[j % 2], 16)

            def bounce(r, first=False):
                sp.wait_ge(gram_act, (r + 1) * chunks)
                sp.wait_ge(gram_dve, (r + 1) * chunks)
                if not first:
                    sp.wait_ge(pairs_loaded, r * 16 * kt_n)
                for q, (i, count_i, back_j, count_j, shift) in stores:
                    sp.dma_start(scratch_entries(i, count_i, back_j, count_j, shift, q),
                                 gram[q * QP + i:q * QP + i + count_i, back_j:back_j + count_j, :, :]
                                 .rearrange("i j a g -> i j (a g)")).then_inc(gram_stored, 16)
                if not first:
                    sp.wait_ge(layer1_done, r * 2)
                sp.wait_ge(gram_stored, (r + 1) * 16 * len(stores))
                for t in range(kt_n):
                    at = first_pair + t * kt_rows
                    sp.dma_start(pairs[:, t, :], scratch[at:at + kt_rows, :]).then_inc(pairs_loaded, 16)

            def store_y(r):
                sp.wait_ge(y_ready, r + 1)
                sp.dma_start(out.rearrange("b o -> o b")[:, bass.ds(r * round_samples, round_samples)],
                             y_row[:, :]).then_inc(y_stored, 16)

            load_idx(0, 0, None)
            load_ids(0, 0, True)
            load_table(0)
            load_table(1)
            load_idx(0, 1, None)
            load_ids(0, 1, True)
            load_x(0, True)
            for j in range(2, picks):
                load_table(j)
            load_ids(1, 0, False)
            for to, of in ((wd[:, :, :], w_dense), (wp[:, :, :], w_pairs), (w2s[:, :, :], w2),
                           (w3s[:, :], w3), (b1s[:, :], b1), (b2s[:, :], b2)):
                sp.dma_start(to, of).then_inc(weights_loaded, 16)
            load_ids(1, 1, False)
            load_idx(1, 0, order_0)

            def round_(r, order=usual, ahead=2):
                load_idx(r + 1, 1, order)
                load_x(r + 1, False)
                bounce(r, order is order_0)
                if ahead > 1:
                    for h in range(ID_LOADS):
                        load_ids(r + 2, h, False)
                    load_idx(r + 2, 0, usual)
                    store_y(r)

            round_(0, order_0)
            with sp.Fori(1, rounds - 2) as r:
                round_(r)
            round_(rounds - 2, ahead=1)
            bounce(rounds - 1)
            store_y(rounds - 2)
            store_y(rounds - 1)
            sp.wait_ge(y_stored, rounds * 16)

        @block.gpsimd
        def _(pool):
            nc.gpsimd.memset(ident[:, :], 0.0).then_inc(ident_cleared, 1)
            for c in tile_counts:
                nc.gpsimd.iota(row_int[c][:, :], [[1, c]], base=0, channel_multiplier=c
                               ).then_inc(row_int_ready, 1)
            pool.wait_ge(ident_cleared, 1)
            nc.gpsimd.affine_select(out=ident[:, :], in_=ident[:, :], compare_op=ALU.not_equal, fill=1.0,
                                    base=0, pattern=[[-1, P]], channel_multiplier=1).then_inc(ident_ready, 1)
            expected = [pool.alloc_register(f"idx_expected{a}") for a in range(BLOCKS)]
            for a in range(BLOCKS):
                pool.reg_mov(expected[a], 16)
            with pool.Fori(0, rounds):
                for a in range(BLOCKS):
                    pool.wait_ge(idx_loaded[a], pool.snap(expected[a]))
                    pool.reg_add(expected[a], expected[a], 16)
                    for f in range(gathers + a):
                        nc.gpsimd.indirect_dma_start(
                            rows[a][:, f, :], None, gather_tables[f],
                            bass.IndirectOffsetOnAxis(idx[a][:, f:f + 1], 0),
                        ).then_inc(gathered[a][f // QUAD], 16)

        @block.tensor
        def _(pe):
            def bank(r, step, order):
                e = order.index(step)
                if e >= 2:
                    pe.wait_ge(emptied, r * len(order) + e - 1)
                elif order is not order_0:
                    pe.wait_ge(emptied, r * len(order))
                return turn_ps[e % 2]

            def pick(r, j, order=usual):
                ps = bank(r, ("pick", j), order)[:, :, :]
                pe.wait_ge(one_hot_ready, r * picks + j + 1)
                if order is order_0:
                    pe.wait_ge(table_lo_ready, j + 1)
                for t in range(pick_tiles[j]):
                    for part in (table_hi[j], table_lo[j]):
                        last = nc.tensor.matmul(
                            ps.rearrange("d a s -> d (a s)")[:, 0:pick_samples(j)],
                            part[0:pick_rows[j], t, :],
                            one_hot[j % AHEAD][0:pick_rows[j], t, 0:pick_samples(j)],
                            start=(t == 0 and part is table_hi[j]),
                            stop=(t == pick_tiles[j] - 1 and part is table_lo[j]))
                last.then_inc(filled, 1)

            def turn(r, a, k, order=usual):
                ps = bank(r, ("turn", a, k), order)
                pe.wait_ge(gathered[a][k], (r + 1) * 16 * len(quad_features(a, k)))
                for j, f in enumerate(quad_features(a, k)):
                    last = nc.tensor.transpose(ps[:, j, :], rows[a][:, f, :], ident[:, :])
                last.then_inc(filled, 1)

            def grams(r, a, c, order=usual):
                m = a * CHUNKS + c
                if c == 0:
                    pe.wait_ge(block_in[a], r + 1)
                if not (order is order_0 and m < 2):
                    pe.wait_ge(gram_act, r * chunks + m - 1)
                    pe.wait_ge(gram_dve, r * chunks + m - 1)
                for g in range(CHUNK):
                    group = turned[a][:, c * CHUNK + g, :, :]
                    last = nc.tensor.matmul(gram_ps[m % 2][0:used, g, 0:NQ * n],
                                            group.rearrange("d q f -> d (q f)")[:, 0:used],
                                            group[:, :, 0:n], start=True, stop=True)
                last.then_inc(gram_done, 1)

            def layer1(r, m, first=False):
                if m == 0:
                    pe.wait_ge(xt_ready, (r + 1) * BLOCKS)
                    pe.wait_ge(pairs_loaded, (r + 1) * 16 * kt_n)
                if not first and m == 0:
                    pe.wait_ge(h2_ready, (r - 1) * m2 + 1)
                if not first and m == 2:
                    pe.wait_ge(y_ready, r)
                cols = slice(m * P, (m + 1) * P)
                o = mlp_ps[m // 2][:, m % 2, :]
                nc.tensor.matmul(o, wds[:, cols], xt[:, :, :, :].rearrange("d q a g -> d (q a g)"),
                                 start=True, stop=False)
                for t in range(kt_n):
                    last = nc.tensor.matmul(o, wp[:, t, cols], pairs[:, t, :],
                                            start=False, stop=(t == kt_n - 1))
                if m % 2:
                    last.then_inc(layer1_done, 1)

            def layer2(r):
                for m in range(m2):
                    for t in range(m1):
                        if m == 0 and t % 2 == 0:
                            pe.wait_ge(h1_ready, r * m1 + t + 2)
                        last = nc.tensor.matmul(mlp_ps[m][:, 0, :], w2s[:, t, m * P:(m + 1) * P],
                                                h1[:, t, :], start=(t == 0), stop=(t == m1 - 1))
                    last.then_inc(layer2_done, 1)

            def layer3(r):
                pe.wait_ge(y_terms_ready, r * m2 + m2)
                nc.tensor.matmul(mlp_ps[1][0:1, 0, :], ones[:, :], y_terms[:, :], start=True, stop=True
                                 ).then_inc(layer3_done, 1)

            def round_(r, order=usual, following=True, layers=True):
                grams(r, 0, 0, order)
                if order is order_0:
                    turn(r, 1, 0, order)
                    turn(r, 1, 1, order)
                else:
                    turn(r, 1, 2)
                    turn(r, 1, 3)
                    if following:
                        layer3(r - 1)
                grams(r, 0, 1, order)
                if order is order_0:
                    turn(r, 1, 2, order)
                elif following:
                    turn(r, 1, 4)
                grams(r, 0, 2, order)
                if order is order_0:
                    turn(r, 1, 3, order)
                grams(r, 0, 3, order)
                if order is order_0 or not following:
                    turn(r, 1, 4, order)
                if order is order_0:
                    pick(r + 1, 0)
                for c in range(CHUNKS):
                    grams(r, 1, c, order)
                if following:
                    for j in range(1 if order is order_0 else 0, picks):
                        pick(r + 1, j)
                if order is order_0:
                    pe.wait_ge(wds_ready, 1)
                    pe.wait_ge(weights_loaded, weight_loads * 16)
                for m in range(m1):
                    if layers:
                        layer1(r, m, order is order_0)
                    if following and m < 2:
                        turn(r + 1, 0, 2 * m)
                        turn(r + 1, 0, 2 * m + 1)
                    elif following and m == 2:
                        turn(r + 1, 0, 4)
                        turn(r + 1, 1, 0)
                    elif following:
                        turn(r + 1, 1, 1)
                if layers:
                    layer2(r)

            pe.wait_ge(ident_ready, 1)
            pe.wait_ge(pad_cleared, BLOCKS)
            pe.wait_ge(ones_ready, 1)
            for kind, *which in order_0[:quads + picks]:
                (pick if kind == "pick" else turn)(0, *which, order_0)
            round_(0, order_0)
            with pe.Fori(1, rounds - 2) as r:
                round_(r)
            round_(rounds - 2, layers=False)
            round_(rounds - 1, following=False, layers=False)
            for r in range(rounds - 2, rounds):
                for m in range(m1):
                    layer1(r, m)
                    if r == rounds - 1 and m == 0:
                        layer3(r - 1)
                layer2(r)
            layer3(rounds - 1)

        def copy_gram(engine, copy, r, a, c, quadrants, first):
            m = a * CHUNKS + c
            engine.wait_ge(gram_done, r * chunks + m + 1)
            if m == 0 and not first:
                engine.wait_ge(gram_stored, r * 16 * len(stores))
            for q in quadrants:
                last = copy(gram[q * QP:q * QP + n, ::-1, a, c * CHUNK:(c + 1) * CHUNK],
                            gram_ps[m % 2][q * QP:q * QP + n, :, q * n:(q + 1) * n]
                            .rearrange("i g j -> i j g"))
            return last

        @block.scalar
        def _(act):
            def relu1(r, bank):
                act.wait_ge(layer1_done, r * 2 + bank + 1)
                for m in range(2 * bank, 2 * bank + 2):
                    nc.scalar.activation(h1[:, m, :], mlp_ps[bank][:, m % 2, :], ACT.Relu,
                                         bias=b1s[:, m:m + 1]).then_inc(h1_ready, 1)

            def relu2(r):
                for m in range(m2):
                    act.wait_ge(layer2_done, r * m2 + m + 1)
                    nc.scalar.activation(h2[:, m, :], mlp_ps[m][:, 0, :], ACT.Relu,
                                         bias=b2s[:, m:m + 1]).then_inc(h2_ready, 1)

            def picked_at(j):
                return 2 + j if j < picks - 1 else 0

            def copy_picked(r, j, order=usual):
                act.wait_ge(filled, passed(r, ("pick", j), order))
                if j == 0 and order is not order_0:
                    for a in range(BLOCKS):
                        act.wait_ge(block_in[a], r)
                count = pick_samples(j) // P
                nc.scalar.copy(picked[:, picked_at(j), 0:count, :],
                               turn_ps[order.index(("pick", j)) % 2][:, 0:count, :]).then_inc(emptied, 1)

            def copy_turned(r, a, k, order=usual):
                act.wait_ge(filled, passed(r, ("turn", a, k), order))
                count = len(quad_features(a, k))
                nc.scalar.copy(
                    turned[a][:, :, :, QUAD * k:QUAD * k + count].rearrange("d g q f -> d f q g"),
                    turn_ps[order.index(("turn", a, k)) % 2][:, 0:count, :]
                    .rearrange("d f (q g) -> d f q g", q=NQ)).then_inc(emptied, 1)

            def complete_block(r, a, order=usual):
                act.wait_ge(emptied, r * len(order) + picks + (a + 1) * quads)
                act.wait_ge(x_loaded, (r + 1) * 16)
                nc.scalar.copy(turned[a][:, :, :, gathers + a:n].rearrange("d g q j -> d j q g"),
                               picked[:, a:, a, :].rearrange("d j (q g) -> d j q g", q=NQ)
                               ).then_inc(block_in[a], 1)

            def keep_x(r):
                for a in range(BLOCKS):
                    act.wait_ge(block_in[a], r + 1)
                    nc.scalar.copy(xt[:, :, a, :], turned[a][:, :, :, gathers + 1].rearrange("d g q -> d q g")
                                   ).then_inc(xt_ready, 1)

            def table_high(j):
                act.wait_ge(staged_loaded[j % 2], 16 * (j // 2 + 1))
                tall, tiles = pick_rows[j], pick_tiles[j]
                nc.scalar.copy(table_hi[j][0:tall, :, :], staged[j % 2][0:tall, 0:tiles, :]
                               ).then_inc(table_hi_ready, 1)

            def grams(r, a, c, order):
                copy_gram(act, nc.scalar.copy, r, a, c, (0, 1), order is order_0).then_inc(gram_act, 1)

            def round_(r, order=usual, following=True, layers=True):
                grams(r, 0, 0, order)
                if order is order_0:
                    copy_turned(r, 1, 0, order)
                    copy_turned(r, 1, 1, order)
                else:
                    copy_turned(r, 1, 2)
                    copy_turned(r, 1, 3)
                grams(r, 0, 1, order)
                if order is order_0:
                    copy_turned(r, 1, 2, order)
                elif following:
                    copy_turned(r, 1, 4)
                    complete_block(r, 1)
                grams(r, 0, 2, order)
                if order is order_0:
                    copy_turned(r, 1, 3, order)
                elif following:
                    keep_x(r)
                grams(r, 0, 3, order)
                if order is order_0 or not following:
                    copy_turned(r, 1, 4, order)
                    complete_block(r, 1, order)
                if order is order_0:
                    keep_x(r)
                    copy_picked(r + 1, 0)
                for c in range(CHUNKS):
                    grams(r, 1, c, order)
                if following:
                    for j in range(1 if order is order_0 else 0, picks):
                        copy_picked(r + 1, j)
                if order is order_0:
                    act.wait_ge(weights_loaded, weight_loads * 16)
                if following:
                    copy_turned(r + 1, 0, 0)
                    copy_turned(r + 1, 0, 1)
                if layers:
                    relu1(r, 0)
                if following:
                    copy_turned(r + 1, 0, 2)
                    copy_turned(r + 1, 0, 3)
                    copy_turned(r + 1, 0, 4)
                    copy_turned(r + 1, 1, 0)
                if layers:
                    relu1(r, 1)
                if following:
                    copy_turned(r + 1, 1, 1)
                    complete_block(r + 1, 0)
                if layers:
                    relu2(r)

            table_high(0)
            table_high(1)
            for kind, *which in order_0[:quads + picks]:
                (copy_picked if kind == "pick" else copy_turned)(0, *which, order_0)
                if kind == "pick" and which[0] + 2 < picks:
                    table_high(which[0] + 2)
            complete_block(0, 0, order_0)
            round_(0, order_0)
            with act.Fori(1, rounds - 2) as r:
                round_(r)
            round_(rounds - 2, layers=False)
            round_(rounds - 1, following=False, layers=False)
            for r in range(rounds - 2, rounds):
                if r == rounds - 1:
                    keep_x(r)
                for bank in range(m1 // 2):
                    relu1(r, bank)
                relu2(r)

        @block.vector
        def _(dve):
            def mark_rows(r, j, order=usual):
                h = j // ids_each
                if j % ids_each == 0:
                    dve.wait_ge(id_rows_loaded[h], (r + 1) * 16)
                if j >= AHEAD:
                    dve.wait_ge(filled, passed(r, ("pick", j - AHEAD), order))
                tall = pick_rows[j]
                for t in range(pick_tiles[j]):
                    last = nc.vector.tensor_scalar(
                        one_hot[j % AHEAD][0:tall, t, 0:pick_samples(j)],
                        id_rows[h][0:tall, j % ids_each, 0:pick_samples(j)],
                        row_of[pick_tiles[j]][0:tall, t:t + 1], None, ALU.is_equal)
                last.then_inc(one_hot_ready, 1)

            def weigh_h2(r):
                dve.wait_ge(h2_ready, r * m2 + 1)
                nc.vector.tensor_scalar(y_terms[:, :], h2[:, 0, :], w3s[:, 0:1], None, ALU.mult
                                        ).then_inc(y_terms_ready, 1)
                dve.wait_ge(h2_ready, r * m2 + 2)
                dve.wait_ge(y_terms_ready, r * m2 + 1)
                nc.vector.scalar_tensor_tensor(y_terms[:, :], h2[:, 1, :], w3s[:, 1:2], y_terms[:, :],
                                               ALU.mult, ALU.add).then_inc(y_terms_ready, 1)

            def copy_y(r, first=False):
                dve.wait_ge(layer3_done, r + 1)
                if not first:
                    dve.wait_ge(y_stored, r * 16)
                nc.vector.tensor_copy(
                    y_row[:, :].rearrange("o (a q g) -> o a q g", a=BLOCKS, q=NQ),
                    mlp_ps[1][0:1, 0, :].rearrange("o (q a g) -> o a q g", q=NQ, a=BLOCKS),
                ).then_inc(y_ready, 1)

            def grams(r, a, c, order):
                copy_gram(dve, nc.vector.tensor_copy, r, a, c, (2, 3), order is order_0
                          ).then_inc(gram_dve, 1)

            def round_(r, order=usual, first_y=False, following=True):
                y_before = order is not order_0 and following
                if y_before:
                    weigh_h2(r - 1)
                for a in range(BLOCKS):
                    for c in range(CHUNKS):
                        grams(r, a, c, order)
                        if a == 0 and c == 0 and y_before:
                            copy_y(r - 1, first_y)
                        if following and c % 2 and 2 * a + c // 2 < AHEAD:
                            mark_rows(r + 1, 2 * a + c // 2)
                if following:
                    for j in range(AHEAD, picks):
                        mark_rows(r + 1, j)

            dve.wait_ge(row_int_ready, len(tile_counts))
            for c in tile_counts:
                nc.vector.tensor_copy(row_of[c][:, :], row_int[c][:, :]).then_inc(row_of_ready, 1)
            nc.vector.memset(ones[:, :], 1.0).then_inc(ones_ready, 1)
            for a in range(BLOCKS):
                nc.vector.memset(turned[a][:, :, :, n:QP], 0.0).then_inc(pad_cleared, 1)
            dve.wait_ge(row_of_ready, len(tile_counts))
            for j in range(picks):
                mark_rows(0, j, order_0)
                dve.wait_ge(table_hi_ready, j + 1)
                tall, tiles = pick_rows[j], pick_tiles[j]
                nc.vector.tensor_tensor(table_lo[j][0:tall, :, :], staged[j % 2][0:tall, 0:tiles, :],
                                        table_hi[j][0:tall, :, :], ALU.subtract).then_inc(table_lo_ready, 1)
            dve.wait_ge(weights_loaded, weight_loads * 16)
            nc.vector.tensor_tensor(wds[:, :], wd[:, 0, :], wd[:, 1, :], ALU.add).then_inc(wds_ready, 1)
            round_(0, order_0)
            round_(1, first_y=True)
            with dve.Fori(2, rounds - 1) as r:
                round_(r)
            round_(rounds - 1, following=False)
            for r in range(rounds - 2, rounds):
                weigh_h2(r)
                copy_y(r)


def kernel(**inputs):
    import concourse.bacc as _bacc
    from concourse.bass_utils import run_bass_kernel_spmd as _run

    ids = np.asarray(inputs["ids"])
    features = ids.shape[1]
    tables = [np.asarray(inputs[f"tbl_{f}"]) for f in range(features)]
    w1 = np.asarray(inputs["W_top1"])
    dense = inputs["r_dense_features"].shape[1]
    gathered, picked = split_features([t.shape[0] for t in tables])

    of_pair = {(f, features): dense + f for f in range(features)}
    row = dense + features
    for i in range(features):
        for j in range(i + 1, features):
            of_pair[i, j] = row
            row += 1
    gathered.append(picked[-1])
    column = [*gathered, features, *picked[:-1]]
    order = [of_pair[tuple(sorted((column[i], column[j])))] for i, j in pair_order(features + 1)]
    tiles = -(-len(order) // P)

    def tiled(a, t):
        return a.reshape(t, a.shape[0] // t, -1).transpose(1, 0, 2)

    def columns(a):
        return np.asarray(a).reshape(-1, P).T

    arrays = {
        "x": inputs["r_dense_features"].reshape(-1, BLOCKS * P, dense).transpose(0, 2, 1),
        "gather_ids": ids[:, gathered],
        "pick_ids": ids[:, picked].reshape(-1, BLOCKS * P, len(picked)).transpose(0, 2, 1),
        **{f"tbl_{f}": t for f, t in enumerate(tables)},
        "w_dense": np.stack([w1[:dense], w1[row:]], axis=1), "w_pairs": tiled(w1[order], tiles),
        "b1": columns(inputs["b_top1"]), "w2": tiled(np.asarray(inputs["W_top2"]), w1.shape[1] // P),
        "b2": columns(inputs["b_top2"]), "w3": columns(inputs["W_top3"]),
    }
    arrays = {k: np.ascontiguousarray(v) for k, v in arrays.items()}
    nc = _bacc.Bacc("TRN2", target_bir_lowering=False, num_devices=1)
    aps = {k: nc.dram_tensor(k, v.shape, mybir.dt.from_np(v.dtype), kind="ExternalInput").ap()
           for k, v in arrays.items()}
    out = nc.dram_tensor("out", (ids.shape[0], 1), F32, kind="ExternalOutput").ap()
    dlrm_tower(nc, aps["x"], aps["gather_ids"], aps["pick_ids"], [aps[f"tbl_{f}"] for f in gathered],
               [aps[f"tbl_{f}"] for f in picked], aps["w_dense"], aps["w_pairs"], aps["b1"], aps["w2"],
               aps["b2"], aps["w3"], out)
    r = _run(nc, [arrays], core_ids=[0])
    return r.results[0]["out"]
```
